# Optimizing a Trainium2 kernel written in Bass

```python
import numpy as np
import jax
import jax.numpy as jnp

def _softmax(x, axis=-1):
    return jax.nn.softmax(x, axis=axis)

def _gelu(x):
    return jax.nn.gelu(x, approximate=True)

def _silu(x):
    return jax.nn.silu(x)

def _sigmoid(x):
    return jax.nn.sigmoid(x)

def _layernorm(x, axis=-1, eps=1e-05):
    m = jnp.mean(x, axis=axis, keepdims=True)
    v = jnp.var(x, axis=axis, keepdims=True)
    return (x - m) / jnp.sqrt(v + eps)

def _scatter_add(tgt, idx, src, axis=0):
    return tgt.at[idx].add(src)

def _segment_sum(src, seg, n):
    return jax.ops.segment_sum(src, seg, n)
kernel_name = 'mk_cond_resid_d1_seqx_r2_bba3f0'

def setup_inputs(seed: int=0):
    np.random.seed(seed)
    _w = jnp.asarray

    def _rec_inputs():
        import jax
        import jax.numpy as jnp
        _rk = jax.random.key(seed)
        x = -0.000125 + 0.9999 * jax.random.normal(jax.random.fold_in(_rk, 1), (16, 512, 512), jnp.float32)
        _lenS = 512 - jax.random.randint(jax.random.fold_in(_rk, 7), (16,), 0, max(1, 512 // 4) + 1, jnp.int32)
        _lenS2 = 512 - jax.random.randint(jax.random.fold_in(_rk, 8), (16,), 0, max(1, 512 // 4) + 1, jnp.int32)
        cond_1024 = -0.00493535 + 1.00056 * jax.random.normal(jax.random.fold_in(_rk, 11), (16, 512), jnp.float32)
        return (x, cond_1024)
    x, cond_1024 = _rec_inputs()

    def _L0_cond_setup():
        import jax, jax.numpy as jnp
        import numpy as np
        import math
        N, T, D, H = (64, 256, 512, 512)
        key = jax.random.key(seed)
        k1, k2, k3, k4 = jax.random.split(key, 4)
        x = jax.random.normal(k1, (N, T, D), dtype=jnp.float32)
        h0 = jax.random.normal(k2, (N, H), dtype=jnp.float32)
        Wx = jax.random.normal(k3, (D, 4 * H), dtype=jnp.float32) / math.sqrt(D)
        Wh = jax.random.normal(k4, (H, 4 * H), dtype=jnp.float32) / math.sqrt(H)
        b = jnp.zeros((4 * H,), dtype=jnp.float32)
        return {'x': x, 'h0': h0, 'Wx': Wx, 'Wh': Wh, 'b': b}
    _L0_cond_all = _L0_cond_setup()
    _L0_cond_in = {k: v for k, v in _L0_cond_all.items() if k in ('Wx', 'Wh', 'b')}
    del _L0_cond_all
    return {'x': x, 'cond_1024': cond_1024, 'L0_cond_Wx': _L0_cond_in['Wx'], 'L0_cond_Wh': _L0_cond_in['Wh'], 'L0_cond_b': _L0_cond_in['b']}

def reference(x, cond_1024, L0_cond_Wx, L0_cond_Wh, L0_cond_b):
    import jax
    import jax.numpy as jnp

    def _L0_cond_ref(x, h0, Wx, Wh, b):
        import jax, jax.numpy as jnp
        import numpy as np
        import math
        N, T, D, H = (64, 256, 512, 512)
        Hdim = h0.shape[1]
        xW = jnp.einsum('ntd,dg->ntg', x, Wx) + b

        def step(carry, xw_t):
            prev_h, prev_c = carry
            a = xw_t + prev_h @ Wh
            i = jax.nn.sigmoid(a[:, :Hdim])
            f = jax.nn.sigmoid(a[:, Hdim:2 * Hdim])
            o = jax.nn.sigmoid(a[:, 2 * Hdim:3 * Hdim])
            g = jnp.tanh(a[:, 3 * Hdim:])
            next_c = f * prev_c + i * g
            next_h = o * jnp.tanh(next_c)
            return ((next_h, next_c), next_h)
        c0 = jnp.zeros_like(h0)
        _, hs = jax.lax.scan(step, (h0, c0), jnp.swapaxes(xW, 0, 1))
        return jnp.swapaxes(hs, 0, 1)
    x = x + _L0_cond_ref(x, cond_1024, L0_cond_Wx, L0_cond_Wh, L0_cond_b)
    return x

_drawn_inputs = setup_inputs


def setup_inputs(seed=0):
    import zlib

    import numpy as np

    out = dict(_drawn_inputs(seed))
    spreads = {'L0_cond_b': (0.0, 0.1)}
    factors = {}
    for name, (base, spread) in spreads.items():
        noise = np.random.default_rng([zlib.crc32(name.encode()), seed]).standard_normal(out[name].shape)
        drawn = base * np.exp(spread * noise) if base else spread * noise
        out[name] = jnp.asarray(drawn.astype(out[name].dtype))
    for name, factor in factors.items():
        out[name] = (out[name] * factor).astype(out[name].dtype)
    return out
```

```python
from contextlib import ExitStack

import concourse.bass as bass
from concourse import mybir

ALU = mybir.AluOpType
ACT = mybir.ActivationFunctionType
AX = mybir.AxisListType
F32 = mybir.dt.float32
F16 = mybir.dt.float16
BF16 = mybir.dt.bfloat16
I32 = mybir.dt.int32
ABSMAX = bass.bass_isa.ReduceOp.absmax
TINY = 2.0 ** -60



def lstm_kernel(nc, x, h0, wx, wh, bias, out):
    B, T, D = x.shape
    H = h0.shape[1]
    G = 4
    Q = 4
    C = D // (Q * 32)
    HALVES = 2
    CC = C // HALVES
    HC = G * CC * 32
    PAIRS = T // 2
    SLOTS = 4
    BODY = 2 * SLOTS
    TURNS = T // BODY
    XCH = 16
    XCOLS = B * T * D // 128 // XCH
    XRING = 4
    assert D == H == 512 and B == 16 and T % BODY == 0

    with ExitStack() as ctx:
        def sb(name, shape, dt):
            return ctx.enter_context(nc.sbuf_tensor(name, shape, dt))

        def sem(name):
            return ctx.enter_context(nc.semaphore(name))

        w_high = {k: sb(f"{k}_high", [128, C, Q * HALVES, G, CC * 32], F16) for k in ("wx", "wh")}
        w_low = {k: sb(f"{k}_low", [128, C, Q * HALVES, G, CC * 32], F16) for k in ("wx", "wh")}
        b_halves = sb("b_halves", [128, Q * HALVES, G, CC * 32], F16)
        bias_unit = sb("bias_unit", [128, 32], BF16)
        w_stage = {k: sb(f"{k}_stage", [128, C, G * H], F32) for k in ("wx", "wh")}
        b_stage = sb("b_stage", [128, G * H], F32)
        x_scan = sb("x_scan", [128, XRING, XCOLS], F32)
        w_tops = sb("w_tops", [128, 2 * C], F32)
        x_tops = sb("x_tops", [128, XCH + 1], F32)
        part_tops = sb("part_tops", [128, 3], F32)
        tops = sb("tops", [128, 3], F32)
        exponent = sb("exponent", [128, 3], I32)
        scale_bits = sb("scale_bits", [128, 3], I32)
        inverse_bits = sb("inverse_bits", [128, 3], I32)
        combined = sb("combined", [128, 4], F32)

        h0_rows = sb("h0_rows", [128, C * 32], F32)
        h0_feat = sb("h0_feat", [128, C, 32], F32)
        x_rows = [sb(f"x_rows{i}", [128, C * 32], F32) for i in range(SLOTS)]
        out_rows = [sb(f"out_rows{i}", [128, C * 32], F32) for i in range(SLOTS)]
        x_feat = [sb(f"x_feat{i}", [128, C * 2, 16], F32) for i in range(2)]
        x_halves = [sb(f"x_halves{i}", [128, C * 2, 2, 16], F16) for i in range(2)]
        h_halves = [sb(f"h_halves{i}", [128, C, 2, 16], F16) for i in range(2)]
        h_feat = [sb(f"h_feat{i}", [128, C, 2, 16], F32) for i in range(2)]
        h_rows = sb("h_rows", [128, C * 32], F32)
        parts = [sb(f"parts{n}", [128, G * CC, 2, 16], F32) for n in range(HALVES)]
        preact = [sb(f"preact{n}", [128, G * CC * 16], F32) for n in range(HALVES)]
        gates = [sb(f"gates{n}", [128, G, CC * 16], F32) for n in range(HALVES)]
        kept = [sb(f"kept{n}", [128, CC * 16], F32) for n in range(HALVES)]
        entering = [sb(f"entering{n}", [128, CC * 16], F32) for n in range(HALVES)]
        o_gate = [sb(f"o_gate{n}", [128, CC, 16], F32) for n in range(HALVES)]
        cell = [sb(f"cell{n}", [128, CC * 16], F32) for n in range(HALVES)]
        cell_tanh = [sb(f"cell_tanh{n}", [128, CC, 16], F32) for n in range(HALVES)]

        acc = [[ctx.enter_context(nc.psum_tensor(f"acc{p}{n}", [128, 512], F32)) for n in range(HALVES)]
               for p in range(2)]

        w_loaded = [sem(f"w_loaded{i}") for i in range(2 * C)]
        b_loaded = sem("b_loaded")
        h0_loaded = sem("h0_loaded")
        scan_loaded = [sem(f"scan_loaded{i}") for i in range(XRING)]
        scan_used = sem("scan_used")
        x_loaded = [sem(f"x_loaded{i}") for i in range(SLOTS)]
        out_free = [sem(f"out_free{i}") for i in range(SLOTS)]
        zeroed = sem("zeroed")
        dve_setup = sem("dve_setup")
        w_part_top = sem("w_part_top")
        w_top = sem("w_top")
        x_part_top = sem("x_part_top")
        x_top = sem("x_top")
        w_scaled = sem("w_scaled")
        w_high_done = sem("w_high_done")
        w_ready = sem("w_ready")
        scales_ready = sem("scales_ready")
        x_turned = sem("x_turned")
        x_high = sem("x_high")
        x_ready = sem("x_ready")
        acc_ready = sem("acc_ready")
        parts_ready = sem("parts_ready")
        preact_ready = sem("preact_ready")
        gates_ready = sem("gates_ready")
        products_ready = sem("products_ready")
        cell_ready = sem("cell_ready")
        cell_tanh_ready = sem("cell_tanh_ready")
        h_feat_ready = sem("h_feat_ready")
        h_ready = sem("h_ready")
        h_turned = sem("h_turned")
        out_ready = sem("out_ready")

        W_, X_, B_ = 0, 1, 2
        w_scale, x_scale, b_scale = (scale_bits[:, i:i + 1].bitcast(F32) for i in (W_, X_, B_))
        w_inverse, x_inverse, b_inverse = (inverse_bits[:, i:i + 1].bitcast(F32) for i in (W_, X_, B_))
        acc_scale, acc_inverse, half_x_scale, unit = (combined[:, i:i + 1] for i in range(4))

        x_pairs = x.rearrange("b (p t) (a h) -> p a t b h", t=2, a=Q)
        out_pairs = out.rearrange("b (p t) (a h) -> p a t b h", t=2, a=Q)
        x_flat = x.rearrange("b t d -> (b t d)").rearrange("(p n) -> p n", p=128)
        w_dram = {"wx": wx.rearrange("(a c r) g -> c a r g", a=Q, c=C),
                  "wh": wh.rearrange("(a c r) g -> c a r g", a=Q, c=C)}
        pieces = [(k, c) for k in ("wx", "wh") for c in range(C)]

        def of_quadrant(tile, a):
            return tile[32 * a:32 * a + 32, :]

        block = ctx.enter_context(nc.Block())

        @block.sync
        def _(sp):
            for n, (k, c) in enumerate(pieces):
                for a in range(Q):
                    sp.dma_start(w_stage[k][32 * a:32 * a + 32, c, :], w_dram[k][c, a]).then_inc(w_loaded[n], 16)
            sp.wait_ge(zeroed, 2)
            for p in range(2):
                sp.dma_start(b_stage[32 * p:32 * p + 1, :], bias.rearrange("(o g) -> o g", o=1))\
                    .then_inc(b_loaded, 16)
            for a in range(Q):
                sp.dma_start(h0_rows[32 * a:32 * a + B, :], h0[:, 128 * a:128 * a + 128]).then_inc(h0_loaded, 16)
            for i in range(XCH):
                if i >= XRING:
                    sp.wait_ge(scan_used, i - XRING + 1)
                sp.dma_start(x_scan[:, i % XRING, :], x_flat[:, i * XCOLS:(i + 1) * XCOLS])\
                    .then_inc(scan_loaded[i % XRING], 16)

            def load(slot, pair):
                for a in range(Q):
                    sp.dma_start(of_quadrant(x_rows[slot], a), x_pairs[pair, a]).then_inc(x_loaded[slot], 16)

            for p in range(SLOTS):
                load(p, p)

            def turn(i, last):
                for j in range(SLOTS):
                    sp.wait_ge(out_ready, i * SLOTS + (j + 1))
                    for a in range(Q):
                        sp.dma_start(out_pairs[i * SLOTS + j, a], of_quadrant(out_rows[j], a))\
                            .then_inc(out_free[j], 16)
                    if not last:
                        load(j, i * SLOTS + (j + SLOTS))

            with sp.Fori(0, TURNS - 1) as i:
                turn(i, False)
            turn(TURNS - 1, True)
            for j in range(SLOTS):
                sp.wait_ge(out_free[j], 16 * Q * TURNS + 1)

        @block.gpsimd
        def _(pool):
            pool.memset(b_stage[:], 0.0).then_inc(zeroed, 1)
            pool.memset(h0_rows[:], 0.0).then_inc(zeroed, 1)
            for j in range(SLOTS):
                pool.memset(out_rows[j][:], 0.0).then_inc(out_free[j], 1)
            pool.wait_ge(w_part_top, 1)
            pool.partition_all_reduce(tops[:, 0:1], part_tops[:, 0:1], 128, ABSMAX).then_inc(w_top, 1)
            pool.wait_ge(x_part_top, 1)
            pool.partition_all_reduce(tops[:, 1:3], part_tops[:, 1:3], 128, ABSMAX).then_inc(x_top, 1)

        @block.scalar
        def _(act):
            for n, (k, c) in enumerate(pieces):
                act.wait_ge(w_scaled, n + 1)
                act.activation(w_high[k][:, c], w_stage[k][:, c, :].rearrange("p (g m q) -> p m g q", g=G, q=CC * 32),
                               ACT.Copy).then_inc(w_high_done, 1)

            def high_of_x(i, j, p):
                act.wait_ge(x_turned, i * SLOTS + (j + 1))
                act.activation(x_halves[p][:, :, 0, :], x_feat[p][:], ACT.Copy, scale=x_scale).then_inc(x_high, 1)

            for j in range(2):
                high_of_x(0, j, j)

            def turn(i, last):
                for s in range(BODY):
                    for n in range(HALVES):
                        act.wait_ge(preact_ready, i * 2 * BODY + (2 * s + n + 1))
                        act.activation(gates[n][:], preact[n][:], ACT.Tanh, scale=acc_inverse).then_inc(gates_ready, 1)
                    for n in range(HALVES):
                        act.wait_ge(cell_ready, i * 2 * BODY + (2 * s + n + 1))
                        act.activation(cell_tanh[n][:], cell[n][:], ACT.Tanh, scale=0.5).then_inc(cell_tanh_ready, 1)
                    if s % 2 and not (last and s // 2 + 2 >= SLOTS):
                        high_of_x(i, s // 2 + 2, (s // 2) % 2)

            with act.Fori(0, TURNS - 1) as i:
                turn(i, False)
            turn(TURNS - 1, True)

        @block.tensor
        def _(pe):
            def add_inputs(par):

                for n in range(HALVES):
                    for a in range(Q):
                        pe.matmul(acc[par[0]][n][32 * a:32 * a + 32, 0:HC], bias_unit[:], b_halves[:, 2 * a + n],
                                  start=True, stop=False, tile_position=(0, 32 * a))
                for n in range(HALVES):
                    for c in range(C):
                        for w in (w_high, w_low):
                            for a in range(Q):
                                pe.matmul(acc[par[0]][n][32 * a:32 * a + 32, 0:HC],
                                          x_halves[par[1]][:, 2 * c + par[0]], w["wx"][:, c, 2 * a + n],
                                          start=False, stop=False, tile_position=(0, 32 * a))

            def add_recurrent(par, n, ks):
                for c in ks:
                    for w in (w_high, w_low):
                        for a in range(Q):
                            last = pe.matmul(acc[par][n][32 * a:32 * a + 32, 0:HC], h_halves[1 - par][:, c],
                                             w["wh"][:, c, 2 * a + n], start=False,
                                             stop=(c == C - 1 and w is w_low), tile_position=(0, 32 * a))
                return last

            pe.wait_ge(w_ready, 2 * C)
            pe.wait_ge(scales_ready, 1)
            pe.wait_ge(x_ready, 1)
            add_inputs((0, 0))

            def turn(i, last):
                for s in range(BODY):
                    par = s % 2
                    pe.wait_ge(h_ready, i * 2 * BODY + (2 * s + 1))
                    add_recurrent(par, 0, (0, 1))
                    add_recurrent(par, 1, (0, 1))
                    pe.wait_ge(h_ready, i * 2 * BODY + (2 * s + 2))
                    add_recurrent(par, 0, (2, 3)).then_inc(acc_ready, 1)
                    add_recurrent(par, 1, (2, 3)).then_inc(acc_ready, 1)
                    if last and s == BODY - 1:
                        continue
                    if par:
                        pe.wait_ge(x_ready, i * SLOTS + ((s + 1) // 2 + 1))
                    add_inputs((1 - par, ((s + 1) // 2) % 2))

            with pe.Fori(0, TURNS - 1) as i:
                turn(i, False)
            turn(TURNS - 1, True)

        @block.vector
        def _(dve):
            count = [0]

            def then(ins):
                count[0] += 1
                ins.then_inc(dve_setup, 1)
                dve.wait_ge(dve_setup, count[0])

            def find_scales(cols):
                then(dve.tensor_scalar(exponent[:, cols], tops[:, cols].bitcast(I32), 0x7F800000, None, ALU.bitwise_and))
                then(dve.tensor_scalar(scale_bits[:, cols], exponent[:, cols], -1.0, float((127 + 14 + 127) << 23),
                                       ALU.mult, ALU.add))
                then(dve.tensor_scalar(inverse_bits[:, cols], exponent[:, cols], float(-(14 << 23)), None, ALU.add))

            for n, (k, c) in enumerate(pieces):
                dve.wait_ge(w_loaded[n], 16 * Q)
                last = dve.tensor_reduce(w_tops[:, n:n + 1], w_stage[k][:, c, :], AX.X, ALU.max, apply_absolute_value=True)
            then(last)
            dve.tensor_reduce(part_tops[:, 0:1], w_tops[:], AX.X, ALU.max).then_inc(w_part_top, 1)
            dve.wait_ge(w_top, 1)
            then(dve.tensor_scalar(tops[:, 0:1], tops[:, 0:1], TINY, None, ALU.max))
            find_scales(slice(0, 1))
            for n, (k, c) in enumerate(pieces):
                dve.tensor_scalar(w_stage[k][:, c, 0:3 * H], w_stage[k][:, c, 0:3 * H], w_scale, 0.5, ALU.mult, ALU.mult)
                dve.tensor_scalar(w_stage[k][:, c, 3 * H:4 * H], w_stage[k][:, c, 3 * H:4 * H], w_scale, None, ALU.mult)\
                    .then_inc(w_scaled, 1)
            for n, (k, c) in enumerate(pieces):
                dve.wait_ge(w_high_done, n + 1)
                dve.tensor_tensor(w_low[k][:, c], w_stage[k][:, c, :].rearrange("p (g m q) -> p m g q", g=G, q=CC * 32),
                                  w_high[k][:, c], ALU.subtract).then_inc(w_ready, 1)
            dve.wait_ge(b_loaded, 32)
            dve.tensor_reduce(part_tops[:, 2:3], b_stage[:], AX.X, ALU.max, apply_absolute_value=True)
            dve.wait_ge(h0_loaded, 16 * Q)
            dve.tensor_reduce(x_tops[:, XCH:XCH + 1], h0_rows[:], AX.X, ALU.max, apply_absolute_value=True)
            for i in range(XCH):
                dve.wait_ge(scan_loaded[i % XRING], 16 * (i // XRING + 1))
                last = dve.tensor_reduce(x_tops[:, i:i + 1], x_scan[:, i % XRING, :], AX.X, ALU.max,
                                         apply_absolute_value=True).then_inc(scan_used, 1)
            dve.wait_ge(scan_used, XCH)
            dve.tensor_reduce(part_tops[:, 1:2], x_tops[:], AX.X, ALU.max).then_inc(x_part_top, 1)
            dve.wait_ge(x_top, 1)
            dve.tensor_scalar(tops[:, 1:2], tops[:, 1:2], 1.0, None, ALU.max)
            then(dve.tensor_scalar(tops[:, 2:3], tops[:, 2:3], TINY, None, ALU.max))
            find_scales(slice(1, 3))
            dve.tensor_scalar(half_x_scale, x_scale, 0.5, None, ALU.mult)
            dve.tensor_tensor(acc_inverse, w_inverse, x_inverse, ALU.mult)
            then(dve.tensor_tensor(acc_scale, w_scale, x_scale, ALU.mult))
            for n in range(HALVES):
                dve.memset(cell[n][:], 0.0)
            then(dve.tensor_tensor(unit, acc_scale, b_inverse, ALU.mult))
            dve.memset(bias_unit[:, 16:32], 0.0)
            dve.tensor_scalar(bias_unit[:, 0:16], cell[0][:, 0:16], unit, None, ALU.add)
            dve.tensor_scalar(b_stage[:, 0:3 * H], b_stage[:, 0:3 * H], b_scale, 0.5, ALU.mult, ALU.mult)
            then(dve.tensor_scalar(b_stage[:, 3 * H:4 * H], b_stage[:, 3 * H:4 * H], b_scale, None, ALU.mult))
            b_view = b_stage[:].rearrange("p (g m q) -> p m g q", g=G, q=CC * 32)
            then(dve.tensor_copy(b_halves[:], b_view))
            then(dve.tensor_tensor(b_halves[32:64], b_view[32:64], b_halves[32:64], ALU.subtract))
            then(dve.transpose(h0_feat[:].rearrange("p c q -> p (c q)"), h0_rows[:]))
            then(dve.tensor_scalar(h0_feat[:], h0_feat[:], x_scale, None, ALU.mult))
            then(dve.tensor_copy(h_halves[1][:, :, 0, :], h0_feat[:, :, 0:16]))
            then(dve.tensor_tensor(h_halves[1][:, :, 1, :], h0_feat[:, :, 0:16], h_halves[1][:, :, 0, :], ALU.subtract))
            dve.memset(parts[0][:], 0.0).then_inc(h_ready, 2)
            dve.memset(parts[1][:], 0.0).then_inc(scales_ready, 1)

            def turn_x(i, j, p, turns):
                dve.wait_ge(x_loaded[j % SLOTS], turns)
                dve.transpose(x_feat[p][:].rearrange("p m b -> p (m b)"), x_rows[j % SLOTS][:]).then_inc(x_turned, 1)

            def low_of_x(i, j, p):
                dve.wait_ge(x_high, i * SLOTS + (j + 1))
                dve.scalar_tensor_tensor(x_halves[p][:, :, 1, :], x_feat[p][:], x_scale, x_halves[p][:, :, 0, :],
                                         ALU.mult, ALU.subtract).then_inc(x_ready, 1)

            for j in range(2):
                turn_x(0, j, j, 16 * Q)
                low_of_x(0, j, j)

            def turn(i, last):
                for s in range(BODY):
                    par, t2, pp = s % 2, s % 2, (s // 2) % 2
                    nth = [i * 2 * BODY + (2 * s + n + 1) for n in range(HALVES)]

                    def turn_parts(n):
                        dve.wait_ge(acc_ready, nth[n])
                        dve.transpose(parts[n][:].rearrange("p m s b -> p (m s b)"), acc[par][n][:, 0:HC])\
                            .then_inc(parts_ready, 1)

                    def add_parts(n):
                        dve.wait_ge(parts_ready, nth[n])
                        dve.tensor_tensor(preact[n][:].rearrange("p (m b) -> p m b", b=16), parts[n][:, :, 0, :],
                                          parts[n][:, :, 1, :], ALU.add).then_inc(preact_ready, 1)

                    def gate_products(n):
                        gi, gf, go, gg = (gates[n][:, g, :] for g in range(G))
                        dve.wait_ge(gates_ready, nth[n])
                        dve.scalar_tensor_tensor(kept[n][:], gf, 1.0, cell[n][:], ALU.add, ALU.mult)
                        dve.scalar_tensor_tensor(entering[n][:], gi, 1.0, gg, ALU.add, ALU.mult)\
                            .then_inc(products_ready, 1)
                        dve.tensor_scalar(o_gate[n][:].rearrange("p c b -> p (c b)"), go, 1.0, half_x_scale, ALU.add, ALU.mult)

                    def new_cell(n):
                        dve.wait_ge(products_ready, nth[n])
                        dve.scalar_tensor_tensor(cell[n][:], kept[n][:], 0.5, entering[n][:], ALU.mult, ALU.add)\
                            .then_inc(cell_ready, 1)

                    def new_h(n):
                        cs = slice(CC * n, CC * n + CC)
                        dve.wait_ge(cell_tanh_ready, nth[n])
                        dve.tensor_tensor(h_halves[par][:, cs, 0, :], o_gate[n][:], cell_tanh[n][:], ALU.mult)
                        dve.tensor_tensor(h_feat[pp][:, cs, t2, :], o_gate[n][:], cell_tanh[n][:], ALU.mult)\
                            .then_inc(h_feat_ready, 1)

                    def low_of_h(n):
                        cs = slice(CC * n, CC * n + CC)
                        dve.wait_ge(h_feat_ready, nth[n])
                        dve.tensor_tensor(h_halves[par][:, cs, 1, :], h_feat[pp][:, cs, t2, :],
                                          h_halves[par][:, cs, 0, :], ALU.subtract).then_inc(h_ready, 1)

                    turn_parts(0)
                    add_parts(0)
                    turn_parts(1)
                    add_parts(1)
                    gate_products(0)
                    new_cell(0)
                    gate_products(1)
                    new_cell(1)
                    new_h(0)
                    low_of_h(0)
                    new_h(1)
                    low_of_h(1)
                    j = s // 2
                    ahead = not (last and j + 2 >= SLOTS)
                    if s % 2 == 0:
                        if ahead:
                            loads = 16 * Q * (i + 1) if j + 2 < SLOTS else 16 * Q * (i + 2)
                            turn_x(i, j + 2, j % 2, loads)
                    else:
                        if ahead:
                            low_of_x(i, j + 2, j % 2)
                        dve.transpose(h_rows[:], h_feat[pp][:].rearrange("p c t b -> p (c t b)")).then_inc(h_turned, 1)
                        dve.wait_ge(out_free[j], i * 16 * Q + 1)
                        dve.wait_ge(h_turned, i * SLOTS + (j + 1))
                        dve.scalar_tensor_tensor(out_rows[j][:], h_rows[:], x_inverse, x_rows[j][:], ALU.mult, ALU.add)\
                            .then_inc(out_ready, 1)

            with dve.Fori(0, TURNS - 1) as i:
                turn(i, False)
            turn(TURNS - 1, True)


_INS = ["x", "cond_1024", "L0_cond_Wx", "L0_cond_Wh", "L0_cond_b"]


def kernel(**inputs):
    import numpy as np
    from concourse import bacc
    from concourse.bass_utils import run_bass_kernel_spmd

    nc = bacc.Bacc("TRN2", target_bir_lowering=False, num_devices=1)
    arrays, args = {}, []
    for name in _INS:
        a = np.ascontiguousarray(inputs[name])
        arrays[f"in_{name}"] = a
        args.append(nc.dram_tensor(f"in_{name}", a.shape, mybir.dt.from_np(a.dtype), kind="ExternalInput").ap())
    shape = arrays["in_x"].shape
    args.append(nc.dram_tensor("out_0", shape, F32, kind="ExternalOutput").ap())
    lstm_kernel(nc, *args)
    r = run_bass_kernel_spmd(nc, [arrays], core_ids=[0])
    return r.results[0]["out_0"]
```

```python
from contextlib import ExitStack

import numpy as np

import concourse.bass as bass
from concourse import mybir

ALU = mybir.AluOpType
ACT = mybir.ActivationFunctionType
AX = mybir.AxisListType
F32 = mybir.dt.float32
F16 = mybir.dt.float16
I32 = mybir.dt.int32
ABSMAX = bass.bass_isa.ReduceOp.absmax
TINY = 2.0 ** -60
H_SCALE = 2.0 ** 13


GROUPS = ((0, 1), (1, 2), (2, 4))
ORDER = "A0 L0 A1 L1 G0 O0 C0 G1 O1 A2 H0 C1 L2 W0 H1 G2 W1 O2 C2 H2 W2"
ACT_ORDER = "g0 g1 t0 t1 g2 t2"


def lstm_kernel(nc, x, h0, wx, wh, bias, out):
    B, T, D = x.shape
    H = h0.shape[1]
    G = 4
    Q = 4
    C = H // (Q * 32)
    STEPS = 16
    PAIRS = STEPS // 2
    CHUNKS = T // STEPS
    COLS = STEPS * B
    RING = 4
    NG = len(GROUPS)
    W_RING = 3
    assert D == H == 512 and B == 16 and T % STEPS == 0 and CHUNKS >= RING

    with ExitStack() as ctx:
        def sb(name, shape, dt):
            return ctx.enter_context(nc.sbuf_tensor(name, shape, dt))

        def psum(name, shape, dt):
            return ctx.enter_context(nc.psum_tensor(name, shape, dt))

        def sem(name):
            return ctx.enter_context(nc.semaphore(name))

        w_stage = sb("w_stage", [128, W_RING, G * H], F32)
        w32 = {k: sb(f"{k}32", [128, C, C, G, 128], F32) for k in ("wx", "wh")}
        wh_high = sb("wh_high", [128, C, C, G, 128], F16)
        wh_low = sb("wh_low", [128, C, C, G, 128], F16)
        w_tops = sb("w_tops", [128, 2 * C], F32)
        part_top = sb("part_top", [128, 1], F32)
        top = sb("top", [128, 1], F32)
        exponent = sb("exponent", [128, 1], I32)
        w_scale_bits = sb("w_scale_bits", [128, 1], I32)
        inverse_bits = sb("inverse_bits", [128, 1], I32)
        w_scale, pre_scale = w_scale_bits[:].bitcast(F32), inverse_bits[:].bitcast(F32)
        b_rows = sb("b_rows", [128, 32], F32)
        b_feat = sb("b_feat", [128, 32], F32)
        b_scaled = sb("b_scaled", [128, G, C], F32)
        h0_rows = sb("h0_rows", [128, C * 32], F32)
        h0_feat = sb("h0_feat", [128, C, 32], F32)

        x_ring = sb("x_ring", [128, RING * PAIRS, C * 32], F32)
        x_stage = [sb(f"x_stage{i}", [128, C * 32], F32) for i in range(2)]
        x_turn = [sb(f"x_turn{i}", [128, C, 32], F32) for i in range(2)]
        x_feat = sb("x_feat", [128, 2 * C, COLS], F32)
        inputs = sb("inputs", [128, 2 * C * G, COLS], F32)
        out_rows = [sb(f"out_rows{j}", [128, C * 32], F32) for j in range(PAIRS)]
        h_halves = [sb(f"h_halves{i}", [128, C, 2, B], F16) for i in range(2)]
        h_feat = [sb(f"h_feat{i}", [128, C, 2, B], F32) for i in range(2)]
        h_rows = sb("h_rows", [128, C * 32], F32)

        def per_group(name, gates):
            return [sb(f"{name}{n}", [128, c1 - c0] + ([G] if gates else []) + [B], F32)
                    for n, (c0, c1) in enumerate(GROUPS)]

        partial = per_group("partial", True)
        preact = per_group("preact", True)
        gates = per_group("gates", True)
        kept = per_group("kept", False)
        entering = per_group("entering", False)
        o_gate = per_group("o_gate", False)
        cell = per_group("cell", False)
        cell_tanh = per_group("cell_tanh", False)

        acc = [[psum(f"acc{p}{n}", [128, 512], F32) for n in range(NG)] for p in range(2)]
        in_acc = [psum(f"in_acc{i}", [128, 512], F32) for i in range(2)]

        w_loaded = [sem(f"w_loaded{i}") for i in range(2 * C)]
        b_loaded = sem("b_loaded")
        h0_loaded = sem("h0_loaded")
        x_loaded = [sem(f"x_loaded{j}") for j in range(PAIRS)]
        out_free = [sem(f"out_free{j}") for j in range(PAIRS)]
        zeroed = sem("zeroed")
        dve_setup = sem("dve_setup")
        part_top_ready = sem("part_top_ready")
        top_ready = sem("top_ready")
        w_tiled = sem("w_tiled")
        w_searched = sem("w_searched")
        w_scaled = sem("w_scaled")
        w_high_done = sem("w_high_done")
        w_low_done = sem("w_low_done")
        h0_ready = sem("h0_ready")
        bias_ready = sem("bias_ready")
        x_staged = sem("x_staged")
        x_turned = sem("x_turned")
        x_ready = sem("x_ready")
        in_acc_ready = sem("in_acc_ready")
        inputs_ready = sem("inputs_ready")
        acc_ready = sem("acc_ready")
        partial_ready = sem("partial_ready")
        preact_ready = sem("preact_ready")
        gates_ready = sem("gates_ready")
        products_ready = sem("products_ready")
        cell_ready = sem("cell_ready")
        cell_tanh_ready = sem("cell_tanh_ready")
        h_feat_ready = sem("h_feat_ready")
        h_ready = sem("h_ready")
        h_turned = sem("h_turned")
        out_ready = sem("out_ready")

        x_pairs = x.rearrange("b (p t) (a h) -> p a t b h", t=2, a=Q)
        out_pairs = out.rearrange("b (p t) (a h) -> p a t b h", t=2, a=Q)
        w_dram = {"wx": wx.rearrange("(a c r) g -> c a r g", a=Q, c=C),
                  "wh": wh.rearrange("(a c r) g -> c a r g", a=Q, c=C)}
        b_dram = bias.rearrange("(g a c r) -> a g c r", g=G, a=Q, c=C)
        pieces = [(k, c) for k in ("wx", "wh") for c in range(C)]

        block = ctx.enter_context(nc.Block())

        @block.sync
        def _(sp):
            def load(chunk, slot, j):
                for a in range(Q):
                    sp.dma_start(x_ring[32 * a:32 * a + 32, bass.ds(slot * PAIRS + j, 1), :],
                                 x_pairs[chunk * PAIRS + j, a]).then_inc(x_loaded[j], 16)

            for n, (k, c) in enumerate(pieces):
                if n >= W_RING:
                    sp.wait_ge(w_tiled, G * (n - W_RING + 1))
                    sp.wait_ge(w_searched, n - W_RING + 1)
                for a in range(Q):
                    sp.dma_start(w_stage[32 * a:32 * a + 32, n % W_RING, :], w_dram[k][c, a]).then_inc(w_loaded[n], 16)
                if n == W_RING - 1:
                    for j in range(PAIRS):
                        load(0, 0, j)
            sp.wait_ge(zeroed, 2)
            for a in range(Q):
                sp.dma_start(b_rows[32 * a:32 * a + G * C, :], b_dram[a]).then_inc(b_loaded, 16)
                sp.dma_start(h0_rows[32 * a:32 * a + B, :], h0[:, 128 * a:128 * a + 128]).then_inc(h0_loaded, 16)
            for j in range(PAIRS):
                sp.wait_ge(x_staged, j + 1)
                load(1, 1, j)
            for j in range(PAIRS):
                sp.wait_ge(x_staged, PAIRS + j + 1)
                load(2, 2, j)

            def turn(i, stage):
                for j in range(PAIRS):
                    sp.wait_ge(out_ready, i * PAIRS + (j + 1))
                    for a in range(Q):
                        sp.dma_start(out_pairs[i * PAIRS + j, a], out_rows[j][32 * a:32 * a + 32, :])\
                            .then_inc(out_free[j], 16)
                    if stage == "steady":
                        load(i + 3, (i + 3) % RING, j)

            with sp.Fori(0, CHUNKS - 3) as i:
                turn(i, "steady")
            for i in range(CHUNKS - 3, CHUNKS):
                turn(i, "end")
            for j in range(PAIRS):
                sp.wait_ge(out_free[j], 16 * Q * CHUNKS + 1)

        @block.gpsimd
        def _(pool):
            pool.memset(b_rows[:], 0.0).then_inc(zeroed, 1)
            pool.memset(h0_rows[:], 0.0).then_inc(zeroed, 1)
            for j in range(PAIRS):
                pool.memset(out_rows[j][:], 0.0).then_inc(out_free[j], 1)

            def stage(chunk, slot, j):
                pool.wait_ge(x_loaded[j], (chunk + 1) * 16 * Q)
                if not (isinstance(chunk, int) and chunk == 0 and j < 2):
                    pool.wait_ge(x_turned, chunk * PAIRS + (j - 1))
                pool.tensor_copy(x_stage[j % 2][:], x_ring[:, bass.ds(slot * PAIRS + j, 1), :])\
                    .then_inc(x_staged, 1)

            def place(chunk, parity, j):
                pool.wait_ge(x_turned, chunk * PAIRS + (j + 1))
                pool.tensor_copy(x_feat[:, bass.ds(parity * C, C), 32 * j:32 * j + 32], x_turn[j % 2][:])\
                    .then_inc(x_ready, 1)

            for j in range(PAIRS):
                stage(0, 0, j)
                place(0, 0, j)
            pool.wait_ge(part_top_ready, 1)
            pool.partition_all_reduce(top[:], part_top[:], 128, ABSMAX).then_inc(top_ready, 1)
            for j in range(PAIRS):
                stage(1, 1, j)
                place(1, 1, j)
            with pool.Fori(0, CHUNKS - 2) as i:
                for j in range(PAIRS):
                    stage(i + 2, (i + 2) % RING, j)
                    place(i + 2, i % 2, j)

        @block.scalar
        def _(act):
            for n, (k, c) in enumerate(pieces):
                act.wait_ge(w_loaded[n], 16 * Q)
                for g in range(G):
                    act.activation(w32[k][:, c, :, g, :].rearrange("p m (a r) -> p m a r", a=Q),
                                   w_stage[:, n % W_RING, g * H:(g + 1) * H].rearrange("p (a m r) -> p m a r", a=Q, r=32),
                                   ACT.Copy).then_inc(w_tiled, 1)
            for c in range(C):
                act.wait_ge(w_scaled, C + c + 1)
                act.activation(wh_high[:, c], w32["wh"][:, c], ACT.Copy).then_inc(w_high_done, 1)
            act.wait_ge(bias_ready, 1)
            scale_of_preact = act.alloc_register("scale_of_preact")
            act.reg_load(scale_of_preact, inverse_bits[0:1, 0:1])

            def input_tile(chunk, parity, m):
                act.wait_ge(in_acc_ready, chunk * C * G + (m + 1))
                act.activation(inputs[:, bass.ds(parity * C * G + m, 1), :], in_acc[m % 2][:, 0:COLS], ACT.Identity,
                               scale=H_SCALE, bias=b_scaled[:, m % G, m // G:m // G + 1]).then_inc(inputs_ready, 1)

            for m in range(C * G):
                input_tile(0, 0, m)

            def turn(i, last):
                for s in range(STEPS):
                    if not last and s:
                        input_tile(i + 1, (i + 1) % 2, s - 1)
                    nth = [i * NG * STEPS + (NG * s + n + 1) for n in range(NG)]

                    def gate_tanh(n):
                        act.wait_ge(preact_ready, nth[n])
                        act.activation(gates[n][:], preact[n][:], ACT.Tanh, scale=scale_of_preact)\
                            .then_inc(gates_ready, 1)

                    def tanh_of_cell(n):
                        act.wait_ge(cell_ready, nth[n])
                        act.activation(cell_tanh[n][:], cell[n][:], ACT.Tanh, scale=0.5).then_inc(cell_tanh_ready, 1)

                    for op in ACT_ORDER.split():
                        {"g": gate_tanh, "t": tanh_of_cell}[op[0]](int(op[1]))
                if not last:
                    input_tile(i + 1, (i + 1) % 2, STEPS - 1)

            with act.Fori(0, CHUNKS - 1) as i:
                turn(i, False)
            turn(CHUNKS - 1, True)

        @block.tensor
        def _(pe):
            def input_tile(chunk, parity, m, first=False):
                cb, g = divmod(m, G)
                if first and m < 2:
                    pass
                elif first:
                    pe.wait_ge(inputs_ready, m - 1)
                else:
                    pe.wait_ge(inputs_ready, chunk * C * G + (m - 1))
                target = in_acc[m % 2]
                for c in range(C):
                    if first and c == C - 1:
                        for ch in range(C):
                            pe.matmul(target[:, 0:B], w32["wh"][:, ch, cb, g, :], h0_feat[:, ch, 0:B],
                                      start=False, stop=False, skip_group_check=True)
                    last = pe.matmul(target[:, 0:COLS], w32["wx"][:, c, cb, g, :],
                                     x_feat[:, bass.ds(parity * C + c, 1), :], start=(c == 0), stop=(c == C - 1))
                last.then_inc(in_acc_ready, 1)

            def recurrent(par, n, ks, opens):
                c0, c1 = GROUPS[n]
                for c in ks:
                    for cb in range(c0, c1):
                        for g in range(G):
                            col = ((cb - c0) * G + g) * 2 * B
                            for w in (wh_high, wh_low):
                                last = pe.matmul(acc[par][n][:, col:col + 2 * B], w[:, c, cb, g, :],
                                                 h_halves[1 - par][:, c], start=(opens and cb == c0 and g == 0 and w is wh_high),
                                                 stop=(c == C - 1 and w is wh_low), skip_group_check=True)
                return last

            pe.wait_ge(x_ready, PAIRS)
            pe.wait_ge(w_scaled, 2 * C)
            pe.wait_ge(h0_ready, 1)
            for m in range(C * G):
                input_tile(0, 0, m, first=True)
            pe.wait_ge(w_low_done, C)

            def turn(i, last):
                for s in range(STEPS):
                    par = s % 2
                    for k in range(NG - 1):
                        pe.wait_ge(h_ready, i * NG * STEPS + (NG * s + k + 1))
                        for n in range(NG):
                            recurrent(par, n, range(*GROUPS[k]), k == 0)
                    pe.wait_ge(h_ready, i * NG * STEPS + (NG * s + NG))
                    for n in range(NG):
                        recurrent(par, n, range(*GROUPS[-1]), False).then_inc(acc_ready, 1)
                    if not last:
                        if s == 0:
                            pe.wait_ge(x_ready, (i + 2) * PAIRS)
                        input_tile(i + 1, (i + 1) % 2, s)

            with pe.Fori(0, CHUNKS - 1) as i:
                turn(i, False)
            turn(CHUNKS - 1, True)

        @block.vector
        def _(dve):
            count = [0]

            def then(ins):
                count[0] += 1
                ins.then_inc(dve_setup, 1)
                dve.wait_ge(dve_setup, count[0])

            def turn_x(i, j):
                dve.wait_ge(x_staged, i * PAIRS + (j + 1))
                if not (isinstance(i, int) and i == 0 and j < 2):
                    dve.wait_ge(x_ready, i * PAIRS + (j - 1))
                dve.transpose(x_turn[j % 2][:].rearrange("p c q -> p (c q)"), x_stage[j % 2][:]).then_inc(x_turned, 1)

            for n, (k, c) in enumerate(pieces):
                dve.wait_ge(w_loaded[n], 16 * Q)
                dve.tensor_reduce(w_tops[:, n:n + 1], w_stage[:, n % W_RING, :], AX.X, ALU.max,
                                         apply_absolute_value=True).then_inc(w_searched, 1)
            dve.wait_ge(w_searched, 2 * C)
            dve.tensor_reduce(part_top[:], w_tops[:], AX.X, ALU.max).then_inc(part_top_ready, 1)
            for j in range(PAIRS):
                turn_x(0, j)
            dve.wait_ge(top_ready, 1)
            then(dve.tensor_scalar(top[:], top[:], TINY, None, ALU.max))
            then(dve.tensor_scalar(exponent[:], top[:].bitcast(I32), 0x7F800000, None, ALU.bitwise_and))
            then(dve.tensor_scalar(w_scale_bits[:], exponent[:], -1.0, float((127 + 14 + 127) << 23), ALU.mult, ALU.add))
            then(dve.tensor_scalar(inverse_bits[:], exponent[:], float(-((14 + 13) << 23)), None, ALU.add))
            for n, (k, c) in enumerate(pieces):
                if n == 0:
                    dve.wait_ge(w_tiled, 2 * C * G)
                dve.tensor_scalar(w32[k][:, c, :, 0:3, :], w32[k][:, c, :, 0:3, :], w_scale, 0.5, ALU.mult, ALU.mult)
                dve.tensor_scalar(w32[k][:, c, :, 3, :], w32[k][:, c, :, 3, :], w_scale, None, ALU.mult)\
                    .then_inc(w_scaled, 1)
            dve.wait_ge(h0_loaded, 16 * Q)
            dve.transpose(h0_feat[:].rearrange("p c q -> p (c q)"), h0_rows[:]).then_inc(h0_ready, 1)
            dve.wait_ge(b_loaded, 16 * Q)
            then(dve.transpose(b_feat[:], b_rows[:]))
            then(dve.tensor_scalar(b_feat[:], b_feat[:], w_scale, H_SCALE, ALU.mult, ALU.mult))
            dve.tensor_scalar(b_scaled[:, 0:3, :].rearrange("p g c -> p (g c)"), b_feat[:, 0:3 * C], 0.5, None, ALU.mult)
            dve.tensor_copy(b_scaled[:, 3, :], b_feat[:, 3 * C:4 * C]).then_inc(bias_ready, 1)
            for c in range(C):
                dve.wait_ge(w_high_done, c + 1)
                dve.tensor_tensor(wh_low[:, c], w32["wh"][:, c], wh_high[:, c], ALU.subtract).then_inc(w_low_done, 1)
            for j in range(PAIRS):
                turn_x(1, j)
            for n in range(NG):
                dve.memset(cell[n][:], 0.0)
            dve.memset(h_halves[1][:], 0.0).then_inc(h_ready, NG)

            def turn(i, last):
                for s in range(STEPS):
                    par, t2, pp = s % 2, s % 2, (s // 2) % 2
                    nth = [i * NG * STEPS + (NG * s + n + 1) for n in range(NG)]

                    def sides(n):
                        c0, c1 = GROUPS[n]
                        view = acc[par][n][:, 0:(c1 - c0) * G * 2 * B].rearrange("p (m s b) -> p m s b", s=2, b=B)
                        return view[:, :, 0, :], view[:, :, 1, :]

                    def flat(t):
                        return t[:].rearrange("p c g b -> p (c g) b")

                    def add_inputs(n):
                        c0, c1 = GROUPS[n]
                        dve.wait_ge(acc_ready, nth[n])
                        dve.tensor_tensor(flat(partial[n]), sides(n)[0],
                                          inputs[:, bass.ds((i % 2) * (C * G) + c0 * G, (c1 - c0) * G), s * B:(s + 1) * B],
                                          ALU.add).then_inc(partial_ready, 1)

                    def add_low(n):
                        dve.wait_ge(partial_ready, nth[n])
                        dve.tensor_tensor(flat(preact[n]), sides(n)[1], flat(partial[n]), ALU.add)\
                            .then_inc(preact_ready, 1)

                    def gate_products(n):
                        gi, gf, gg = (gates[n][:, :, g, :] for g in (0, 1, 3))
                        dve.wait_ge(gates_ready, nth[n])
                        dve.scalar_tensor_tensor(kept[n][:], gf, 1.0, cell[n][:], ALU.add, ALU.mult)
                        dve.scalar_tensor_tensor(entering[n][:], gi, 1.0, gg, ALU.add, ALU.mult)\
                            .then_inc(products_ready, 1)

                    def output_gate(n):
                        dve.tensor_scalar(o_gate[n][:], gates[n][:, :, 2, :], 1.0, 0.5 * H_SCALE, ALU.add, ALU.mult)

                    def new_cell(n):
                        dve.wait_ge(products_ready, nth[n])
                        dve.scalar_tensor_tensor(cell[n][:], kept[n][:], 0.5, entering[n][:], ALU.mult, ALU.add)\
                            .then_inc(cell_ready, 1)

                    def new_h(n):
                        cs = slice(*GROUPS[n])
                        dve.wait_ge(cell_tanh_ready, nth[n])
                        dve.tensor_tensor(h_halves[par][:, cs, 0, :], o_gate[n][:], cell_tanh[n][:], ALU.mult)
                        dve.tensor_tensor(h_feat[pp][:, cs, t2, :], o_gate[n][:], cell_tanh[n][:], ALU.mult)\
                            .then_inc(h_feat_ready, 1)

                    def low_of_h(n):
                        cs = slice(*GROUPS[n])
                        dve.wait_ge(h_feat_ready, nth[n])
                        dve.tensor_tensor(h_halves[par][:, cs, 1, :], h_feat[pp][:, cs, t2, :],
                                          h_halves[par][:, cs, 0, :], ALU.subtract).then_inc(h_ready, 1)

                    if s == 0:
                        dve.wait_ge(inputs_ready, (i + 1) * C * G)
                    stages = dict(A=add_inputs, L=add_low, G=gate_products, O=output_gate, C=new_cell, H=new_h, W=low_of_h)
                    for op in ORDER.split():
                        stages[op[0]](int(op[1]))
                    j = s // 2
                    if s % 2 == 0:
                        if stage_ahead(i, last):
                            turn_x(i + 2, j)
                    else:
                        dve.transpose(h_rows[:], h_feat[pp][:].rearrange("p c t b -> p (c t b)")).then_inc(h_turned, 1)
                        dve.wait_ge(out_free[j], i * 16 * Q + 1)
                        dve.wait_ge(h_turned, i * PAIRS + (j + 1))
                        dve.scalar_tensor_tensor(out_rows[j][:], h_rows[:], 1.0 / H_SCALE,
                                                 x_ring[:, bass.ds((i % RING) * PAIRS + j, 1), :].rearrange("p o q -> p (o q)"),
                                                 ALU.mult, ALU.add).then_inc(out_ready, 1)

            def stage_ahead(i, last):
                return not last

            with dve.Fori(0, CHUNKS - 2) as i:
                turn(i, False)
            for i in (CHUNKS - 2, CHUNKS - 1):
                turn(i, True)


_INS = ["x", "cond_1024", "L0_cond_Wx", "L0_cond_Wh", "L0_cond_b"]


def kernel(**inputs):
    import numpy as np
    from concourse import bacc
    from concourse.bass_utils import run_bass_kernel_spmd

    nc = bacc.Bacc("TRN2", target_bir_lowering=False, num_devices=1)
    arrays, args = {}, []
    for name in _INS:
        a = np.ascontiguousarray(inputs[name])
        arrays[f"in_{name}"] = a
        args.append(nc.dram_tensor(f"in_{name}", a.shape, mybir.dt.from_np(a.dtype), kind="ExternalInput").ap())
    shape = arrays["in_x"].shape
    args.append(nc.dram_tensor("out_0", shape, F32, kind="ExternalOutput").ap())
    lstm_kernel(nc, *args)
    r = run_bass_kernel_spmd(nc, [arrays], core_ids=[0])
    return r.results[0]["out_0"]
```

```python
from contextlib import ExitStack

import concourse.bass as bass
from concourse import mybir

ALU = mybir.AluOpType
ACT = mybir.ActivationFunctionType
AX = mybir.AxisListType
F32 = mybir.dt.float32
F16 = mybir.dt.float16
I32 = mybir.dt.int32
TINY = 2.0 ** -60
H_SCALE = 2.0 ** 13


GROUPS = ((0, 1), (1, 2), (2, 4))
PLACED = (0, 1)
ORDER = "A0 A1 G0 O0 C0 G1 O1 A2 H0 C1 L2 W0 H1 G2 W1 O2 C2 H2 W2"
X_SCALE_FROM = 4
X_TOP_STEP = X_SCALE_FROM + 4
ACT_ORDER = "p0 p1 g0 g1 t0 t1 g2 t2"


def INPUT_PRODUCTS(w_high, w_low, high, low):
    return ((w_high, high), (w_high, low), (w_low, high))


def lstm_kernel(nc, x, h0, wx, wh, bias, out):
    B, T, D = x.shape
    H = h0.shape[1]
    G = 4
    Q = 4
    C = H // (Q * 32)
    STEPS = 16
    PAIRS = STEPS // 2
    CHUNKS = T // STEPS
    COLS = STEPS * B
    RING = 4
    NG = len(GROUPS)
    W_RING = 3
    assert D == H == 512 and B == 16 and T % STEPS == 0 and CHUNKS >= RING and CHUNKS % 2 == 0

    with ExitStack() as ctx:
        def sb(name, shape, dt):
            return ctx.enter_context(nc.sbuf_tensor(name, shape, dt))

        def psum(name, shape, dt):
            return ctx.enter_context(nc.psum_tensor(name, shape, dt))

        def sem(name):
            return ctx.enter_context(nc.semaphore(name))

        w_stage = sb("w_stage", [128, W_RING, G * H], F32)
        w32 = {k: sb(f"{k}32", [128, C, C, G, 128], F32) for k in ("wx", "wh")}
        wh_high = sb("wh_high", [128, C, C, G, 128], F16)
        wh_low = sb("wh_low", [128, C, C, G, 128], F16)
        stage_halves = w_stage[:].rearrange("p w n -> p (w n)").bitcast(F16).rearrange("p (w n) -> p w n", n=G * H)
        spent_halves = w32["wx"][:, 0:2 * (C - W_RING)].rearrange("p k m g n -> p (k m g n)").bitcast(F16)\
            .rearrange("p (w n) -> p w n", n=G * H)
        places = [stage_halves[:, n] for n in range(2 * W_RING)] + [spent_halves[:, 2 * n] for n in range(2 * (C - W_RING))]
        places = [p.rearrange("p (m g n) -> p m g n", m=C, g=G) for p in places]
        wx_high, wx_low = places[:C], places[C:]
        w_tops = sb("w_tops", [128, 2, C], F32)
        part_top = sb("part_top", [128, 3], F32)
        w_bound = sb("w_bound", [128, 3], F32)
        w_exponent = sb("w_exponent", [128, 3], I32)
        w_scale_bits = sb("w_scale_bits", [128, 3], I32)
        inverse_bits = sb("inverse_bits", [128, 3], I32)
        wx_scale, wh_scale, h0_scale = (w_scale_bits[:, n:n + 1].bitcast(F32) for n in range(3))
        acc_scale = sb("acc_scale", [128, 1], F32)
        pre_bits = sb("pre_bits", [128, 1], I32)
        rescale = sb("rescale", [128, 1], F32)
        x_tops = sb("x_tops", [128, 4], F32)
        x_top = sb("x_top", [128, 1], F32)
        x_bound = sb("x_bound", [128, 1], F32)
        x_exponent = sb("x_exponent", [128, 1], I32)
        x_scale_bits = sb("x_scale_bits", [128, 2], I32)
        x_inverse_bits = sb("x_inverse_bits", [128, 2], I32)
        in_scale = sb("in_scale", [128, 2], F32)
        ones = sb("ones", [128, 128], F32)
        b_rows = sb("b_rows", [128, 32], F32)
        b_feat = sb("b_feat", [128, 32], F32)
        b_halved = sb("b_halved", [128, G, C], F32)
        b_scaled = sb("b_scaled", [128, G, C], F32)
        h0_rows = sb("h0_rows", [128, C * 32], F32)
        h0_feat = sb("h0_feat", [128, C, 32], F32)
        h0_halves = sb("h0_halves", [128, C, 2, B], F16)
        h0_sums = sb("h0_sums", [128, C * G, B], F32)
        h0_rescale = sb("h0_rescale", [128, 1], F32)

        x_ring = sb("x_ring", [128, RING * PAIRS, C * 32], F32)
        x_chunk = sb("x_chunk", [128, PAIRS, C * 32], F32)
        x_turn = [sb(f"x_turn{i}", [128, C, 32], F32) for i in range(2)]
        x_high = sb("x_high", [128, 2 * C, COLS], F16)
        x_low = sb("x_low", [128, 2 * C, COLS], F16)
        inputs = sb("inputs", [128, 2 * C * G, COLS], F32)
        first_x = [inputs[:, (C * G) + n * C:(C * G) + (n + 1) * C, :] for n in range(2)]
        out_rows = [sb(f"out_rows{i}", [128, PAIRS // 2, C * 32], F32) for i in range(2)]
        h_halves = [sb(f"h_halves{i}", [128, C, 2, B], F16) for i in range(2)]
        h_feat = [sb(f"h_feat{i}", [128, C, 2, B], F32) for i in range(2)]
        h_rows = sb("h_rows", [128, C * 32], F32)

        def per_group(name, gates):
            return [sb(f"{name}{n}", [128, c1 - c0] + ([G] if gates else []) + [B], F32)
                    for n, (c0, c1) in enumerate(GROUPS)]

        partial = per_group("partial", True)
        preact = per_group("preact", True)
        gates = per_group("gates", True)
        kept = per_group("kept", False)
        entering = per_group("entering", False)
        o_gate = per_group("o_gate", False)
        cell = per_group("cell", False)
        cell_tanh = per_group("cell_tanh", False)

        acc = [[psum(f"acc{p}{n}", [128, 512], F32) for n in range(NG)] for p in range(2)]
        in_acc = [psum(f"in_acc{i}", [128, 512], F32) for i in range(2)]
        w_sum = acc[0][0][:, 0:3]
        x_sums = {k: bank[:, 0:1] for k, bank in ((1, acc[0][1]), (2, acc[0][2]), ("later", in_acc[0]))}

        def parts(par, n):
            c0, c1 = GROUPS[n]
            return acc[par][n][:, 0:(c1 - c0) * G * 3 * B].rearrange("p (m s b) -> p m s b", s=3, b=B)

        h0_part = acc[1][0][:].rearrange("p (m s b) -> p m s b", s=2, b=B)

        w_loaded = [sem(f"w_loaded{i}") for i in range(2 * C)]
        b_loaded = sem("b_loaded")
        h0_loaded = sem("h0_loaded")
        x_loaded = sem("x_loaded")
        out_free = [sem(f"out_free{i}") for i in range(2)]
        zeroed = sem("zeroed")
        dve_setup = sem("dve_setup")
        part_top_ready = sem("part_top_ready")
        w_sum_ready = sem("w_sum_ready")
        ones_ready = sem("ones_ready")
        x_tops_ready = sem("x_tops_ready")
        x_top_ready = sem("x_top_ready")
        x_sum_ready = sem("x_sum_ready")
        x_bound_ready = sem("x_bound_ready")
        x_exponent_ready = sem("x_exponent_ready")
        x_scale_ready = sem("x_scale_ready")
        in_scale_ready = sem("in_scale_ready")
        x_scaled = sem("x_scaled")
        x_high_ready = sem("x_high_ready")
        first_x_turned = sem("first_x_turned")
        wx_high_done = sem("wx_high_done")
        wx_low_done = sem("wx_low_done")
        w_tiled = sem("w_tiled")
        w_searched = sem("w_searched")
        w_scale_ready = sem("w_scale_ready")
        w_high_done = sem("w_high_done")
        w_low_done = sem("w_low_done")
        h0_turned = sem("h0_turned")
        h0_high_done = sem("h0_high_done")
        h0_ready = sem("h0_ready")
        h0_part_ready = sem("h0_part_ready")
        early_inputs_scaled = sem("early_inputs_scaled")
        first_inputs_ready = sem("first_inputs_ready")
        bias_ready = sem("bias_ready")
        x_staged = sem("x_staged")
        x_turned = sem("x_turned")
        x_ready = sem("x_ready")
        in_acc_ready = sem("in_acc_ready")
        inputs_ready = sem("inputs_ready")
        inputs_placed = sem("inputs_placed")
        acc_ready = sem("acc_ready")
        partial_ready = sem("partial_ready")
        preact_ready = sem("preact_ready")
        gates_ready = sem("gates_ready")
        products_ready = sem("products_ready")
        cell_ready = sem("cell_ready")
        cell_tanh_ready = sem("cell_tanh_ready")
        h_feat_ready = sem("h_feat_ready")
        h_ready = sem("h_ready")
        h_turned = sem("h_turned")
        out_ready = sem("out_ready")

        x_pairs = x.rearrange("b (p t) (a h) -> a t b p h", t=2, a=Q)
        out_pairs = out.rearrange("b (p t) (a h) -> a t b p h", t=2, a=Q)
        w_dram = {"wx": wx.rearrange("(a c r) g -> c a r g", a=Q, c=C),
                  "wh": wh.rearrange("(a c r) g -> c a r g", a=Q, c=C)}
        b_dram = bias.rearrange("(g a c r) -> a g c r", g=G, a=Q, c=C)
        pieces = [(k, c) for k in ("wx", "wh") for c in range(C)]

        block = ctx.enter_context(nc.Block())

        def load_x(eng, chunk, slot):
            for a in range(Q):
                for t in range(2):
                    row = 32 * a + B * t
                    eng.dma_start(x_ring[row:row + B, bass.ds(slot * PAIRS, PAIRS), :],
                                  x_pairs[a, t, :, bass.ds(chunk * PAIRS, PAIRS), :]).then_inc(x_loaded, 16)

        X_LOAD = STORE = 2 * Q * 16

        @block.sync
        def _(sp):
            for n, (k, c) in enumerate(pieces):
                if n >= W_RING:
                    sp.wait_ge(w_tiled, G * (n - W_RING + 1))
                    sp.wait_ge(w_searched, n - W_RING + 1)
                sp.dma_start(w_stage[:, n % W_RING, :], w_dram[k][c]).then_inc(w_loaded[n], 16)
                if n == C - 1:
                    sp.wait_ge(zeroed, 2)
                    for a in range(Q):
                        sp.dma_start(b_rows[32 * a:32 * a + G * C, :], b_dram[a]).then_inc(b_loaded, 16)
                        sp.dma_start(h0_rows[32 * a:32 * a + B, :], h0[:, 128 * a:128 * a + 128]).then_inc(h0_loaded, 16)
            for chunk in range(1, RING):
                sp.wait_ge(x_loaded, X_LOAD * chunk)
                load_x(sp, chunk, chunk)

            def turn(i, ahead):
                for half in range(2):
                    sp.wait_ge(out_ready, i * PAIRS + (half + 1) * PAIRS // 2)
                    for a in range(Q):
                        for t in range(2):
                            row = 32 * a + B * t
                            sp.dma_start(out_pairs[a, t, :, bass.ds(i * PAIRS + half * PAIRS // 2, PAIRS // 2), :],
                                         out_rows[half][row:row + B]).then_inc(out_free[half], 16)
                if ahead:
                    load_x(sp, i + RING, i % RING)

            with sp.Fori(0, CHUNKS - RING) as i:
                turn(i, True)
            for i in range(CHUNKS - RING, CHUNKS):
                turn(i, False)
            for half in range(2):
                sp.wait_ge(out_free[half], STORE * CHUNKS + 1)

        @block.gpsimd
        def _(pool):
            pool.memset(b_rows[:], 0.0).then_inc(zeroed, 1)
            pool.memset(h0_rows[:], 0.0).then_inc(zeroed, 1)
            pool.memset(ones[:], 1.0).then_inc(ones_ready, 1)
            for half in range(2):
                pool.memset(out_rows[half][:], 0.0).then_inc(out_free[half], 1)
            pool.wait_ge(x_scale_ready, 1)
            pool.wait_ge(first_x_turned, 2 * PAIRS)
            pool.wait_ge(w_scale_ready, 1)
            pool.tensor_tensor(in_scale[:, 1:2], x_inverse_bits[:, 1:2].bitcast(F32), rescale[:], ALU.mult)\
                .then_inc(in_scale_ready, 1)
            pool.wait_ge(in_scale_ready, 1)
            pool.tensor_scalar(first_x[1], first_x[1], x_scale_bits[:, 1:2].bitcast(F32), None, ALU.mult)\
                .then_inc(x_scaled, PAIRS)
            pool.wait_ge(x_scaled, PAIRS)
            pool.tensor_copy(x_high[:, C:2 * C, :], first_x[1]).then_inc(x_high_ready, PAIRS)
            pool.wait_ge(x_high_ready, PAIRS)
            pool.tensor_tensor(x_low[:, C:2 * C, :], first_x[1], x_high[:, C:2 * C, :], ALU.subtract)\
                .then_inc(x_ready, PAIRS)

            def halves_of_x(done, par):
                pool.wait_ge(x_loaded, (done + 3) * X_LOAD)
                pool.wait_ge(x_turned, done * PAIRS + 1)
                pool.tensor_copy(x_chunk[:], x_ring[:, bass.ds((done + 2) % RING * PAIRS, PAIRS), :]).then_inc(x_staged, 1)
                scale = x_scale_bits[:, par:par + 1].bitcast(F32).unsqueeze(2).to_broadcast([128, C, 32])
                pool.wait_ge(x_scale_ready, done + 2)
                pool.wait_ge(inputs_ready, (done + 1) * C * G)
                pool.tensor_tensor(in_scale[:, par:par + 1], x_inverse_bits[:, par:par + 1].bitcast(F32), rescale[:],
                                   ALU.mult).then_inc(in_scale_ready, 1)
                pool.wait_ge(in_scale_ready, done + 2)
                for j in range(PAIRS):
                    high, low = (h[:, par * C:(par + 1) * C, 32 * j:32 * j + 32] for h in (x_high, x_low))
                    pool.wait_ge(x_turned, done * PAIRS + (j + 2))
                    pool.tensor_tensor(high, x_turn[j % 2][:], scale, ALU.mult).then_inc(x_high_ready, 1)
                    pool.wait_ge(x_high_ready, (done + 1) * PAIRS + (j + 1))
                    pool.tensor_tensor(x_turn[j % 2][:], x_turn[j % 2][:], scale, ALU.mult).then_inc(x_scaled, 1)
                    pool.wait_ge(x_scaled, (done + 1) * PAIRS + (j + 1))
                    pool.tensor_tensor(low, x_turn[j % 2][:], high, ALU.subtract).then_inc(x_ready, 1)

            with pool.Fori(0, (CHUNKS - 2) // 2) as i:
                for par in range(2):
                    halves_of_x(2 * i + par, par)

        @block.scalar
        def _(act):
            load_x(act, 0, 0)

            def tile(n):
                k, c = pieces[n]
                act.wait_ge(w_loaded[n], 16)
                for g in range(G):
                    act.activation(w32[k][:, c, :, g, :].rearrange("p m (a r) -> p m a r", a=Q),
                                   w_stage[:, n % W_RING, g * H:(g + 1) * H].rearrange("p (a m r) -> p m a r", a=Q, r=32),
                                   ACT.Copy, scale=1.0 if g == 3 else 0.5).then_inc(w_tiled, 1)

            def input_tile(chunk, parity, m, scale, b):
                act.wait_ge(in_acc_ready, chunk * C * G + (m + 1))
                act.activation(inputs[:, bass.ds(parity * C * G + m, 1), :], in_acc[m % 2][:, 0:COLS], ACT.Identity,
                               scale=scale, bias=b[:, m % G, m // G:m // G + 1]).then_inc(inputs_ready, 1)

            for n in range(C):
                tile(n)
            act.wait_ge(bias_ready, 1)
            for c in range(C):
                tile(C + c)
                for m in (2 * c, 2 * c + 1):
                    input_tile(0, 0, m, 1.0, b_halved)
            act.wait_ge(w_scale_ready, 1)
            for c in range(C):
                act.activation(wh_high[:, c], w32["wh"][:, c], ACT.Copy, scale=wh_scale).then_inc(w_high_done, 1)
                input_tile(0, 0, 2 * C + 2 * c, acc_scale[:], b_scaled)
                act.activation(wx_high[c], w32["wx"][:, c], ACT.Copy, scale=wx_scale).then_inc(wx_high_done, 1)
                input_tile(0, 0, 2 * C + 2 * c + 1, acc_scale[:], b_scaled)
            def place_inputs(n, s, parity):
                c0, c1 = GROUPS[n]
                act.activation(parts(s % 2, n)[:, :, 2, :],
                               inputs[:, bass.ds(parity * C * G + c0 * G, (c1 - c0) * G), s * B:(s + 1) * B],
                               ACT.Identity).then_inc(inputs_placed, 1)

            act.wait_ge(first_inputs_ready, 1)
            for n in PLACED:
                place_inputs(n, 0, 0)
            scale_of_preact = act.alloc_register("scale_of_preact")
            act.reg_load(scale_of_preact, pre_bits[0:1, 0:1])

            def turn(i, last):
                for s in range(STEPS):
                    if not last and s == STEPS - 1:
                        act.wait_ge(inputs_ready, (i + 1) * C * G + GROUPS[max(PLACED)][1] * G)
                    if not last and s:
                        input_tile(i + 1, (i + 1) % 2, s - 1, in_scale[:, bass.ds((i + 1) % 2, 1)], b_scaled)
                    nth = [i * NG * STEPS + (NG * s + n + 1) for n in range(NG)]

                    def gate_tanh(n):
                        act.wait_ge(preact_ready, nth[n])
                        act.activation(gates[n][:], preact[n][:], ACT.Tanh, scale=scale_of_preact)\
                            .then_inc(gates_ready, 1)

                    def tanh_of_cell(n):
                        act.wait_ge(cell_ready, nth[n])
                        act.activation(cell_tanh[n][:], cell[n][:], ACT.Tanh, scale=0.5).then_inc(cell_tanh_ready, 1)

                    def place_next(n):
                        if n not in PLACED or last and s == STEPS - 1:
                            return
                        if s == STEPS - 1:
                            place_inputs(n, 0, (i + 1) % 2)
                        else:
                            place_inputs(n, s + 1, i % 2)

                    for op in ACT_ORDER.split():
                        {"g": gate_tanh, "t": tanh_of_cell, "p": place_next}[op[0]](int(op[1]))
                if not last:
                    input_tile(i + 1, (i + 1) % 2, STEPS - 1, in_scale[:, bass.ds((i + 1) % 2, 1)], b_scaled)

            with act.Fori(0, CHUNKS - 1) as i:
                turn(i, False)
            turn(CHUNKS - 1, True)

        @block.tensor
        def _(pe):
            def first_input_tile(m):
                if m >= 2:
                    pe.wait_ge(inputs_ready, m - 1)
                for c in range(C):
                    last = pe.matmul(in_acc[m % 2][:, 0:COLS], w32["wx"][:, c, m // G, m % G, :], first_x[0][:, c, :],
                                     start=(c == 0), stop=(c == C - 1))
                last.then_inc(in_acc_ready, 1)

            def input_tile(chunk, parity, m):
                pe.wait_ge(inputs_ready, chunk * C * G + (m - 1))
                for c in range(C):
                    high, low = (x[:, bass.ds(parity * C + c, 1), :] for x in (x_high, x_low))
                    w_high, w_low = (w[c][:, m // G, m % G, :] for w in (wx_high, wx_low))
                    for w, part in INPUT_PRODUCTS(w_high, w_low, high, low):
                        last = pe.matmul(in_acc[m % 2][:, 0:COLS], w, part, start=(c == 0 and w is w_high and part is high),
                                         stop=(c == C - 1 and w is w_low and part is high))
                last.then_inc(in_acc_ready, 1)

            def sum_of_x_top(chunk, x_sum):
                pe.wait_ge(x_top_ready, chunk)
                pe.matmul(x_sum, ones[:], x_top[:], start=True, stop=True).then_inc(x_sum_ready, 1)

            def recurrent(par, n, ks, opens):
                c0, c1 = GROUPS[n]
                for c in ks:
                    for cb in range(c0, c1):
                        for g in range(G):
                            m = (cb - c0) * G + g
                            for w in (wh_high, wh_low):
                                last = pe.matmul(parts(par, n)[:, m, 0:2, :], w[:, c, cb, g, :], h_halves[1 - par][:, c],
                                                 start=(opens and m == 0 and w is wh_high),
                                                 stop=(c == C - 1 and w is wh_low), skip_group_check=True)
                return last

            pe.wait_ge(first_x_turned, PAIRS)
            pe.wait_ge(w_tiled, C * G)
            for m in range(C * G):
                first_input_tile(m)
                if m == C * G // 2:
                    pe.wait_ge(part_top_ready, 2)
                    pe.wait_ge(ones_ready, 1)
                    pe.matmul(w_sum, ones[:], part_top[:], start=True, stop=True).then_inc(w_sum_ready, 1)
            sum_of_x_top(1, x_sums[1])
            pe.wait_ge(h0_ready, 1)
            pe.wait_ge(w_low_done, C)
            for m in range(C * G):
                for c in range(C):
                    for w in (wh_high, wh_low):
                        last = pe.matmul(h0_part[:, m], w[:, c, m // G, m % G, :], h0_halves[:, c],
                                         start=(c == 0 and w is wh_high), stop=(c == C - 1 and w is wh_low))
            last.then_inc(h0_part_ready, 1)
            sum_of_x_top(2, x_sums[2])
            pe.wait_ge(x_bound_ready, 2)
            pe.wait_ge(first_inputs_ready, 1)

            def turn(i, more):
                for s in range(STEPS):
                    par = s % 2
                    if more >= 3 and s == X_TOP_STEP + 2:
                        pe.wait_ge(inputs_ready, (i + 1) * C * G + (X_TOP_STEP + 1))
                        sum_of_x_top(i + 3, x_sums["later"])
                    if PLACED:
                        pe.wait_ge(inputs_placed, i * STEPS * len(PLACED) + (s + 1) * len(PLACED))
                    for k in range(NG - 1):
                        pe.wait_ge(h_ready, i * NG * STEPS + (NG * s + k + 1))
                        for n in range(NG):
                            recurrent(par, n, range(*GROUPS[k]), k == 0)
                    pe.wait_ge(h_ready, i * NG * STEPS + (NG * s + NG))
                    for n in range(NG):
                        recurrent(par, n, range(*GROUPS[-1]), False).then_inc(acc_ready, 1)
                    if more >= 1:
                        if s == 0:
                            pe.wait_ge(x_ready, (i + 1) * PAIRS)
                            pe.wait_ge(wx_low_done, C)
                        if more >= 3 and s == X_TOP_STEP + 2:
                            pe.wait_ge(x_bound_ready, i + 3)
                        input_tile(i + 1, (i + 1) % 2, s)

            with pe.Fori(0, CHUNKS - 3) as i:
                turn(i, 3)
            for i in range(CHUNKS - 3, CHUNKS):
                turn(i, CHUNKS - 1 - i)

        @block.vector
        def _(dve):
            count = [0]

            def then(ins):
                count[0] += 1
                ins.then_inc(dve_setup, 1)
                dve.wait_ge(dve_setup, count[0])

            def turn_first_x(chunk):
                dve.wait_ge(x_loaded, (chunk + 1) * X_LOAD)
                for j in range(PAIRS):
                    dve.transpose(first_x[chunk][:, :, 32 * j:32 * j + 32], x_ring[:, chunk * PAIRS + j, :])\
                        .then_inc(first_x_turned, 1)

            def search_w(pieces_of_w):
                for n in pieces_of_w:
                    k, c = divmod(n, C)
                    dve.wait_ge(w_loaded[n], 16)
                    dve.tensor_reduce(w_tops[:, k, c:c + 1], w_stage[:, n % W_RING, :], AX.X, ALU.max,
                                      apply_absolute_value=True).then_inc(w_searched, 1)

            def x_quarters(k, q, n):
                if q == 0:
                    dve.wait_ge(x_loaded, (k + 1) * X_LOAD)
                pairs = PAIRS // 4
                dve.tensor_reduce(x_tops[:, q:q + n], x_ring[:, bass.ds(k % RING * PAIRS + pairs * q, pairs * n), :]
                                  .rearrange("p (n j) q -> p n (j q)", n=n), AX.X, ALU.max,
                                  apply_absolute_value=True).then_inc(x_tops_ready, n)

            def x_top_of(k):
                dve.wait_ge(x_tops_ready, 4 * k)
                dve.tensor_reduce(x_top[:], x_tops[:], AX.X, ALU.max).then_inc(x_top_ready, 1)

            def x_bound_of(k):
                dve.wait_ge(x_sum_ready, k)
                dve.tensor_scalar(x_bound[:], x_sums[k if isinstance(k, int) and k < 3 else "later"], TINY, None, ALU.max).then_inc(x_bound_ready, 1)

            def x_exponent_of(k):
                dve.wait_ge(x_bound_ready, k)
                dve.tensor_scalar(x_exponent[:], x_bound[:].bitcast(I32), 0x7F800000, None, ALU.bitwise_and)\
                    .then_inc(x_exponent_ready, 1)

            def x_scale_of(k):
                dve.wait_ge(x_exponent_ready, k)
                if not (isinstance(k, int) and k < 3):
                    dve.wait_ge(x_ready, (k - 2) * PAIRS)
                slot = bass.ds(k % 2, 1)
                dve.tensor_scalar(x_scale_bits[:, slot], x_exponent[:], -1.0, float((127 + 14 + 127) << 23), ALU.mult, ALU.add)
                dve.tensor_scalar(x_inverse_bits[:, slot], x_exponent[:], float(-(14 << 23)), None, ALU.add)\
                    .then_inc(x_scale_ready, 1)

            search_w(range(0, 2))
            turn_first_x(0)
            search_w(range(2, C))
            dve.wait_ge(b_loaded, 16 * Q)
            then(dve.transpose(b_feat[:], b_rows[:]))
            dve.tensor_scalar(b_halved[:, 0:3, :].rearrange("p g c -> p (g c)"), b_feat[:, 0:3 * C], 0.5, None, ALU.mult)
            dve.tensor_copy(b_halved[:, 3, :], b_feat[:, 3 * C:4 * C]).then_inc(bias_ready, 1)
            dve.wait_ge(h0_loaded, 16 * Q)
            dve.tensor_reduce(part_top[:, 2:3], h0_rows[:], AX.X, ALU.max, apply_absolute_value=True).then_inc(part_top_ready, 1)
            dve.transpose(h0_feat[:].rearrange("p c q -> p (c q)"), h0_rows[:]).then_inc(h0_turned, 1)
            search_w(range(C, 2 * C))
            dve.wait_ge(w_searched, 2 * C)
            dve.tensor_reduce(part_top[:, 0:2], w_tops[:], AX.X, ALU.max).then_inc(part_top_ready, 1)
            dve.wait_ge(w_sum_ready, 1)
            then(dve.tensor_scalar(w_bound[:], w_sum, TINY, None, ALU.max))
            then(dve.tensor_scalar(w_exponent[:], w_bound[:].bitcast(I32), 0x7F800000, None, ALU.bitwise_and))
            dve.tensor_scalar(w_scale_bits[:], w_exponent[:], -1.0, float((127 + 14 + 127) << 23), ALU.mult, ALU.add)
            dve.tensor_scalar(pre_bits[:], w_exponent[:, 1:2], float(-((14 + 13) << 23)), None, ALU.add)
            then(dve.tensor_scalar(inverse_bits[:], w_exponent[:], float(-(14 << 23)), None, ALU.add))
            then(dve.tensor_scalar(acc_scale[:], wh_scale, H_SCALE, None, ALU.mult))
            dve.tensor_scalar(b_scaled[:], b_halved[:], acc_scale[:], None, ALU.mult)
            dve.tensor_tensor(rescale[:], inverse_bits[:, 0:1].bitcast(F32), acc_scale[:], ALU.mult).then_inc(w_scale_ready, 1)
            dve.tensor_scalar(h0_rescale[:], inverse_bits[:, 2:3].bitcast(F32), H_SCALE, None, ALU.mult)
            dve.wait_ge(h0_turned, 1)
            dve.tensor_scalar(h0_halves[:, :, 0, :], h0_feat[:, :, 0:B], h0_scale, None, ALU.mult).then_inc(h0_high_done, 1)
            dve.wait_ge(h0_high_done, 1)
            dve.scalar_tensor_tensor(h0_halves[:, :, 1, :], h0_feat[:, :, 0:B], h0_scale, h0_halves[:, :, 0, :],
                                     ALU.mult, ALU.subtract).then_inc(h0_ready, 1)
            dve.wait_ge(inputs_ready, 2 * C)
            dve.tensor_scalar(inputs[:, 0:2 * C, :], inputs[:, 0:2 * C, :], acc_scale[:], None, ALU.mult)\
                .then_inc(early_inputs_scaled, 1)
            for c in range(C):
                dve.wait_ge(w_high_done, c + 1)
                dve.scalar_tensor_tensor(wh_low[:, c], w32["wh"][:, c], wh_scale, wh_high[:, c], ALU.mult, ALU.subtract)\
                    .then_inc(w_low_done, 1)
                if c == 2 * (C - W_RING):
                    dve.wait_ge(in_acc_ready, C * G)
                dve.wait_ge(wx_high_done, c + 1)
                if c >= 2 * (C - W_RING):
                    dve.wait_ge(wx_low_done, c - 1)
                dve.scalar_tensor_tensor(wx_low[c], w32["wx"][:, c], wx_scale, wx_high[c], ALU.mult, ALU.subtract)\
                    .then_inc(wx_low_done, 1)
                if c == 1:
                    turn_first_x(1)
                    x_quarters(1, 0, 4)
                    x_top_of(1)
            def x_scale_stages(k):
                x_bound_of(k)
                x_exponent_of(k)
                x_scale_of(k)

            x_scale_stages(1)
            x_quarters(2, 0, 4)
            x_top_of(2)
            dve.wait_ge(h0_part_ready, 1)
            then(dve.tensor_reduce(h0_sums[:], h0_part.rearrange("p m s b -> p m b s"), AX.X, ALU.add))
            dve.wait_ge(inputs_ready, C * G)
            dve.wait_ge(early_inputs_scaled, 1)
            dve.scalar_tensor_tensor(inputs[:, 0:C * G, 0:B], h0_sums[:], h0_rescale[:], inputs[:, 0:C * G, 0:B],
                                     ALU.mult, ALU.add).then_inc(first_inputs_ready, 1)
            x_scale_stages(2)
            dve.wait_ge(first_inputs_ready, 1)
            for n in range(NG):
                dve.memset(cell[n][:], 0.0)
            dve.memset(h_halves[1][:], 0.0).then_inc(h_ready, NG)
            dve.memset(x_turn[0][:], 0.0).then_inc(x_turned, 1)

            def turn_x(i, j):
                if j == 0:
                    dve.wait_ge(x_staged, i - 1)
                if not (isinstance(i, int) and j < 2):
                    dve.wait_ge(x_ready, (i - 1) * PAIRS + (j - 1))
                dve.transpose(x_turn[j % 2][:].rearrange("p c q -> p (c q)"), x_chunk[:, j, :]).then_inc(x_turned, 1)

            def turn(i, more):
                for s in range(STEPS):
                    par, t2, pp = s % 2, s % 2, (s // 2) % 2
                    nth = [i * NG * STEPS + (NG * s + n + 1) for n in range(NG)]

                    summed = [n for n in range(NG) if n not in PLACED]
                    nth_of_dve = {n: i * len(summed) * STEPS + (len(summed) * s + k + 1) for k, n in enumerate(summed)}

                    def flat(t):
                        return t[:].rearrange("p c g b -> p (c g) b")

                    def add_parts(n):
                        dve.tensor_reduce(flat(preact[n]), parts(par, n).rearrange("p m s b -> p m b s"), AX.X, ALU.add)\
                            .then_inc(preact_ready, 1)

                    def add_inputs(n):
                        c0, c1 = GROUPS[n]
                        dve.wait_ge(acc_ready, nth[n])
                        if n in PLACED:
                            return add_parts(n)
                        dve.tensor_tensor(flat(partial[n]), parts(par, n)[:, :, 0, :],
                                          inputs[:, bass.ds((i % 2) * (C * G) + c0 * G, (c1 - c0) * G), s * B:(s + 1) * B],
                                          ALU.add).then_inc(partial_ready, 1)

                    def add_low(n):
                        dve.wait_ge(partial_ready, nth_of_dve[n])
                        dve.tensor_tensor(flat(preact[n]), parts(par, n)[:, :, 1, :], flat(partial[n]), ALU.add)\
                            .then_inc(preact_ready, 1)

                    def gate_products(n):
                        gi, gf, gg = (gates[n][:, :, g, :] for g in (0, 1, 3))
                        dve.wait_ge(gates_ready, nth[n])
                        dve.scalar_tensor_tensor(kept[n][:], gf, 1.0, cell[n][:], ALU.add, ALU.mult)
                        dve.scalar_tensor_tensor(entering[n][:], gi, 1.0, gg, ALU.add, ALU.mult)\
                            .then_inc(products_ready, 1)

                    def output_gate(n):
                        dve.tensor_scalar(o_gate[n][:], gates[n][:, :, 2, :], 1.0, 0.5 * H_SCALE, ALU.add, ALU.mult)

                    def new_cell(n):
                        dve.wait_ge(products_ready, nth[n])
                        dve.scalar_tensor_tensor(cell[n][:], kept[n][:], 0.5, entering[n][:], ALU.mult, ALU.add)\
                            .then_inc(cell_ready, 1)

                    def new_h(n):
                        cs = slice(*GROUPS[n])
                        dve.wait_ge(cell_tanh_ready, nth[n])
                        dve.tensor_tensor(h_halves[par][:, cs, 0, :], o_gate[n][:], cell_tanh[n][:], ALU.mult)
                        dve.tensor_tensor(h_feat[pp][:, cs, t2, :], o_gate[n][:], cell_tanh[n][:], ALU.mult)\
                            .then_inc(h_feat_ready, 1)

                    def low_of_h(n):
                        cs = slice(*GROUPS[n])
                        dve.wait_ge(h_feat_ready, nth[n])
                        dve.tensor_tensor(h_halves[par][:, cs, 1, :], h_feat[pp][:, cs, t2, :],
                                          h_halves[par][:, cs, 0, :], ALU.subtract).then_inc(h_ready, 1)

                    if s == 0:
                        dve.wait_ge(inputs_ready, (i + 1) * C * G)
                    stages = dict(A=add_inputs, L=add_low, G=gate_products, O=output_gate, C=new_cell, H=new_h, W=low_of_h)
                    for op in ORDER.split():
                        stages[op[0]](int(op[1]))
                    j = s // 2
                    if s % 2 == 0:
                        if more >= 2:
                            turn_x(i + 2, j)
                    else:
                        dve.transpose(h_rows[:], h_feat[pp][:].rearrange("p c t b -> p (c t b)")).then_inc(h_turned, 1)
                        half, k = divmod(j, PAIRS // 2)
                        if k == 0:
                            dve.wait_ge(out_free[half], i * STORE + 1)
                        dve.wait_ge(h_turned, i * PAIRS + (j + 1))
                        dve.scalar_tensor_tensor(out_rows[half][:, k, :], h_rows[:], 1.0 / H_SCALE,
                                                 x_ring[:, bass.ds((i % RING) * PAIRS + j, 1), :].rearrange("p o q -> p (o q)"),
                                                 ALU.mult, ALU.add).then_inc(out_ready, 1)
                    if more >= 3:
                        if X_SCALE_FROM <= s < X_SCALE_FROM + 4:
                            x_quarters(i + 3, s - X_SCALE_FROM, 1)
                        for stage, at in ((x_top_of, X_TOP_STEP), (x_bound_of, X_TOP_STEP + 1), (x_exponent_of, X_TOP_STEP + 2),
                                          (x_scale_of, X_TOP_STEP + 3)):
                            if s == at:
                                stage(i + 3)

            with dve.Fori(0, CHUNKS - 3) as i:
                turn(i, 3)
            for i in range(CHUNKS - 3, CHUNKS):
                turn(i, CHUNKS - 1 - i)


_INS = ["x", "cond_1024", "L0_cond_Wx", "L0_cond_Wh", "L0_cond_b"]


def kernel(**inputs):
    import numpy as np
    from concourse import bacc
    from concourse.bass_utils import run_bass_kernel_spmd

    nc = bacc.Bacc("TRN2", target_bir_lowering=False, num_devices=1)
    arrays, args = {}, []
    for name in _INS:
        a = np.ascontiguousarray(inputs[name])
        arrays[f"in_{name}"] = a
        args.append(nc.dram_tensor(f"in_{name}", a.shape, mybir.dt.from_np(a.dtype), kind="ExternalInput").ap())
    shape = arrays["in_x"].shape
    args.append(nc.dram_tensor("out_0", shape, F32, kind="ExternalOutput").ap())
    lstm_kernel(nc, *args)
    r = run_bass_kernel_spmd(nc, [arrays], core_ids=[0])
    return r.results[0]["out_0"]
```
